# Optimizing a Trainium2 kernel written in Bass

```python
import numpy as np
import jax
import jax.numpy as jnp

def _softmax(x, axis=-1):
    return jax.nn.softmax(x, axis=axis)

def _gelu(x):
    return jax.nn.gelu(x, approximate=True)

def _silu(x):
    return jax.nn.silu(x)

def _sigmoid(x):
    return jax.nn.sigmoid(x)

def _layernorm(x, axis=-1, eps=1e-05):
    m = jnp.mean(x, axis=axis, keepdims=True)
    v = jnp.var(x, axis=axis, keepdims=True)
    return (x - m) / jnp.sqrt(v + eps)

def _scatter_add(tgt, idx, src, axis=0):
    return tgt.at[idx].add(src)

def _segment_sum(src, seg, n):
    return jax.ops.segment_sum(src, seg, n)
kernel_name = 'mk_cond_resid_d1_seqx_r4_2a48d8'

def setup_inputs(seed: int=0):
    np.random.seed(seed)
    _w = jnp.asarray

    def _rec_inputs():
        import jax
        import jax.numpy as jnp
        _rk = jax.random.key(seed)
        x = -0.000125 + 0.9999 * jax.random.normal(jax.random.fold_in(_rk, 1), (8, 256, 1024), jnp.float32)
        _lenS = 256 - jax.random.randint(jax.random.fold_in(_rk, 7), (8,), 0, max(1, 256 // 4) + 1, jnp.int32)
        _lenS2 = 256 - jax.random.randint(jax.random.fold_in(_rk, 8), (8,), 0, max(1, 256 // 4) + 1, jnp.int32)
        itok_B_0_23 = jax.random.randint(jax.random.fold_in(_rk, 11), (8,), 0, 24, jnp.int32)
        return (x, itok_B_0_23)
    x, itok_B_0_23 = _rec_inputs()

    def _L0_cond_setup():
        import jax, jax.numpy as jnp
        import numpy as np
        R = 16
        ALPHA = 32
        SCALING = ALPHA / R
        SLOTS = 32
        IN_F = 1024
        OUT_F = 1024
        B, T = (8, 256)
        key = jax.random.key(seed)
        k1, k2, k3, k4, k5, k6 = jax.random.split(key, 6)
        x = jax.random.normal(k1, (B, T, IN_F), dtype=jnp.float32)
        adapter_mapping = jax.random.randint(k2, (B,), 0, SLOTS, dtype=jnp.int32)
        W = jax.random.normal(k3, (OUT_F, IN_F), dtype=jnp.float32) * 0.02
        b = jax.random.normal(k4, (OUT_F,), dtype=jnp.float32) * 0.02
        lora_As = jax.random.normal(k5, (SLOTS, IN_F, R), dtype=jnp.float32) * 0.02
        lora_Bs = jax.random.normal(k6, (SLOTS, R, OUT_F), dtype=jnp.float32) * 0.02
        return {'x': x, 'adapter_mapping': adapter_mapping, 'W': W, 'b': b, 'lora_As': lora_As, 'lora_Bs': lora_Bs}
    _L0_cond_all = _L0_cond_setup()
    _L0_cond_in = {k: v for k, v in _L0_cond_all.items() if k in ('W', 'b', 'lora_As', 'lora_Bs')}
    del _L0_cond_all
    return {'x': x, 'itok_B_0_23': itok_B_0_23, 'L0_cond_W': _L0_cond_in['W'], 'L0_cond_b': _L0_cond_in['b'], 'L0_cond_lora_As': _L0_cond_in['lora_As'], 'L0_cond_lora_Bs': _L0_cond_in['lora_Bs']}

def reference(x, itok_B_0_23, L0_cond_W, L0_cond_b, L0_cond_lora_As, L0_cond_lora_Bs):
    import jax
    import jax.numpy as jnp

    def _L0_cond_ref(x, adapter_mapping, W, b, lora_As, lora_Bs):
        import jax, jax.numpy as jnp
        import numpy as np
        R = 16
        ALPHA = 32
        SCALING = ALPHA / R
        SLOTS = 32
        IN_F = 1024
        OUT_F = 1024
        B, T = (8, 256)
        base_out = jnp.einsum('bti,oi->bto', x, W) + b
        A = lora_As[adapter_mapping]
        Bm = lora_Bs[adapter_mapping]
        lora_h = jnp.einsum('bti,bir->btr', x, A)
        lora_out = jnp.einsum('btr,bro->bto', lora_h, Bm)
        return base_out + lora_out * SCALING
    x = x + _L0_cond_ref(x, itok_B_0_23, L0_cond_W, L0_cond_b, L0_cond_lora_As, L0_cond_lora_Bs)
    return x

_drawn_inputs = setup_inputs


def setup_inputs(seed=0):
    import zlib

    import numpy as np

    out = dict(_drawn_inputs(seed))
    spreads = {}
    factors = {'L0_cond_b': 3.577}
    for name, (base, spread) in spreads.items():
        noise = np.random.default_rng([zlib.crc32(name.encode()), seed]).standard_normal(out[name].shape)
        drawn = base * np.exp(spread * noise) if base else spread * noise
        out[name] = jnp.asarray(drawn.astype(out[name].dtype))
    for name, factor in factors.items():
        out[name] = (out[name] * factor).astype(out[name].dtype)
    return out
```

```python
from contextlib import ExitStack

import concourse.bass as bass
import numpy as np
from concourse import mybir
from concourse.alu_op_type import AluOpType as ALU

F32 = mybir.dt.float32
F32R = mybir.dt.float32r
I32 = mybir.dt.int32
U32 = mybir.dt.uint32
ACT = mybir.ActivationFunctionType

P = 128
BATCH, T, D = 8, 256, 1024
SLOTS, R = 32, 16
SCALING = 32 / R
TILES = D // P
HALF = TILES // 2
N = 512
ROWS = N // T
CHUNKS = BATCH * T // N
Q = 32
PAIR = 2
BANK = [0, 1, 2, 3, 4, 5, 6, 4]
GRANT = TILES


def lora_linear_kernel(nc, x, idx, w, bias, lora_a, lora_b, out):
    with ExitStack() as ctx:
        def sb(name, shape, dt=F32):
            return ctx.enter_context(nc.sbuf_tensor(name, shape, dt))

        def sem(name):
            return ctx.enter_context(nc.semaphore(name))

        x_sb = sb("x_sb", [P, 2, TILES, N])
        x_hi = sb("x_hi", [P, 2, TILES, N], F32R)
        x_lo = sb("x_lo", [P, 2, TILES, N], F32R)
        w_raw = x_sb[:, 1, :, :]
        w_hi = sb("w_hi", [P, TILES, D], F32R)
        w_lo = sb("w_lo", [P, TILES, D], F32R)
        bias_sb = sb("bias_sb", [P, TILES])
        a_raw = sb("a_raw", [P, BATCH, TILES * R])
        a_cols = sb("a_cols", [P, ROWS, TILES, P], F32R)
        b_raw = sb("b_raw", [P, ROWS, D])
        b_rows = sb("b_rows", [P, 2, ROWS, D], F32R)
        hs = sb("hs", [P, N], F32R)
        idx_sb = sb("idx_sb", [P, BATCH], I32)
        lane = sb("lane", [P, 1], I32)
        lane_r = sb("lane_r", [P, 1], I32)
        a_at = sb("a_at", [P, BATCH], U32)
        b_at = sb("b_at", [P, BATCH], U32)
        acc = [ctx.enter_context(nc.psum_tensor(f"acc{n}", [P, N], F32)) for n in range(7)]
        h = ctx.enter_context(nc.psum_tensor("h", [P, N], F32))

        x0_loaded = [sem(f"x0_loaded{k}") for k in range(TILES)]
        x_loaded = sem("x_loaded")
        w_loaded = [sem(f"w_loaded{k}") for k in range(TILES)]
        bias_loaded = sem("bias_loaded")
        idx_loaded = sem("idx_loaded")
        lane_made = sem("lane_made")
        lane_r_made = sem("lane_r_made")
        at_made = sem("at_made")
        a_gathered = [sem(f"a_gathered{b}") for b in range(BATCH)]
        b_gathered = [sem(f"b_gathered{b}") for b in range(ROWS)]
        w_hi_done = sem("w_hi_done")
        w_lo_done = sem("w_lo_done")
        x_hi_done = sem("x_hi_done")
        x_lo_done = sem("x_lo_done")
        a_hi_done = sem("a_hi_done")
        a_lo_done = sem("a_lo_done")
        b_hi_done = sem("b_hi_done")
        b_lo_done = sem("b_lo_done")
        h_done = sem("h_done")
        hs_hi_done = sem("hs_hi_done")
        hs_lo_done = sem("hs_lo_done")
        acc_done = sem("acc_done")
        drained = sem("drained")
        stored = sem("stored")

        def a_part(row, part):
            return a_cols[:, row, :, :].rearrange("p k (q s r) -> p k q s r", q=4, s=PAIR)[:, :, :, part, :]

        def a_source(b):
            return a_raw[:, b, :].rearrange("p (k a r) -> p k a r", k=TILES, a=1).to_broadcast([P, TILES, 4, R])

        def w_piece(tile, half, k):
            return tile[:, k, half * HALF * P:(half + 1) * HALF * P]

        block = ctx.enter_context(nc.Block())

        @block.sync
        def _(sp):
            for k in range(TILES):
                sp.dma_start(w_raw[:, k, :], w[0, k]).then_inc(w_loaded[k], 16)
                sp.dma_start(x_sb[:, 0, k, :], x[0, :, k * N:(k + 1) * N]).then_inc(x0_loaded[k], 16)
            for k in range(TILES):
                sp.wait_ge(w_hi_done, k + 1)
                sp.wait_ge(w_lo_done, k + 1)
                sp.dma_start(w_raw[:, k, :], w[1, k]).then_inc(w_loaded[k], 16)
            sp.wait_ge(w_hi_done, 2 * TILES)
            sp.wait_ge(w_lo_done, 2 * TILES)
            sp.dma_start(x_sb[:, 1, :, :], x[1]).then_inc(x_loaded, 16)

            def store(c, buf):
                for j in range(TILES):
                    sp.wait_ge(drained, c * TILES + (GRANT + j + 1))
                    sp.dma_start(out[bass.ds(c, 1), :, j * N:(j + 1) * N], x_sb[:, bass.ds(buf, 1), j, :]
                                 ).then_inc(stored, 16)

            with sp.Fori(0, 2) as c:
                sp.wait_ge(x_loaded, (c + 1) * 16)
                store(c, c)
                sp.wait_ge(stored, (c + 1) * (16 * TILES))
                sp.dma_start(x_sb[:, bass.ds(c, 1), :, :], x[bass.ds(c + 2, 1)]).then_inc(x_loaded, 16)
            with sp.Fori(2, CHUNKS) as c:
                store(c, c - 2)
            sp.wait_ge(stored, CHUNKS * TILES * 16)

        @block.gpsimd
        def _(pool):
            nc.gpsimd.iota(lane[:], [[0, 1]], base=0, channel_multiplier=1).then_inc(lane_made, 1)

            def gather_b(c):
                if c >= 1:
                    pool.wait_ge(b_hi_done, c * ROWS)
                    pool.wait_ge(b_lo_done, c * ROWS)
                for row in range(ROWS):
                    b = c * ROWS + row
                    pool.indirect_dma_start(b_raw[:, row, :], None, lora_b,
                                            bass.IndirectOffsetOnAxis(ap=b_at[:, b:b + 1], axis=0)
                                            ).then_inc(b_gathered[row], 16)

            pool.wait_ge(at_made, 2)
            for b in range(BATCH):
                pool.indirect_dma_start(a_raw[:, b, :], None, lora_a,
                                        bass.IndirectOffsetOnAxis(ap=a_at[:, b:b + 1], axis=0)
                                        ).then_inc(a_gathered[b], 16)
                if b == ROWS - 1:
                    gather_b(0)

            for c in range(CHUNKS):
                if c == 0:
                    for b in range(BATCH):
                        pool.wait_ge(a_gathered[b], 16)
                for row in range(ROWS):
                    pool.wait_ge(b_gathered[row], 16 * (c + 1))
                if c >= 1:
                    pool.wait_ge(x_lo_done, c * TILES)
                    pool.wait_ge(x_loaded, 16 * c)
                    if c >= 2:
                        pool.wait_ge(acc_done, (c - 1) * TILES)
                    for k in range(TILES):
                        pool.wait_ge(x_hi_done, c * TILES + k + 1)
                        nc.gpsimd.tensor_tensor(x_lo[:, c % 2, k, :], x_sb[:, c % 2, k, :],
                                                x_hi[:, c % 2, k, :].bitcast(F32), ALU.subtract
                                                ).then_inc(x_lo_done, 1)
                for row in range(ROWS):
                    b = c * ROWS + row
                    pool.wait_ge(a_hi_done, b + 1)
                    nc.gpsimd.tensor_tensor(a_part(row, 1), a_source(b), a_part(row, 0).bitcast(F32),
                                            ALU.subtract).then_inc(a_lo_done, 1)
                for row in range(ROWS):
                    b = c * ROWS + row
                    if row == 0:
                        pool.wait_ge(a_lo_done, (c + 1) * ROWS)
                    pool.wait_ge(b_hi_done, b + 1)
                    nc.gpsimd.tensor_tensor(b_rows[2 * Q:, c % 2, row, :], b_raw[2 * Q:, row, :],
                                            b_rows[2 * Q:, c % 2, row, :].bitcast(F32), ALU.subtract
                                            ).then_inc(b_lo_done, 1)
                if c + 1 < CHUNKS:
                    gather_b(c + 1)

        @block.scalar
        def _(act):
            act.dma_start(idx_sb[:], idx.to_broadcast([P, BATCH])).then_inc(idx_loaded, 16)
            act.dma_start(bias_sb[:], bias).then_inc(bias_loaded, 16)

            def w_high(half, k):
                act.wait_ge(w_loaded[k], 16 * (half + 1))
                nc.scalar.activation(w_piece(w_hi, half, k), w_raw[:, k, :], ACT.Copy).then_inc(w_hi_done, 1)

            def x_high(buf, k):
                nc.scalar.activation(x_hi[:, buf, k, :], x_sb[:, buf, k, :],
                                     ACT.Copy).then_inc(x_hi_done, 1)

            for k in range(TILES):
                w_high(0, k)
                act.wait_ge(x0_loaded[k], 16)
                x_high(0, k)
            for row in range(ROWS):
                act.wait_ge(a_gathered[row], 16)
                nc.scalar.activation(a_part(row, 0), a_source(row), ACT.Copy).then_inc(a_hi_done, 1)
            for k in range(TILES):
                w_high(1, k)

            def b_high(c, buf):
                for row in range(ROWS):
                    act.wait_ge(b_gathered[row], (c + 1) * 16)
                    nc.scalar.activation(b_rows[:, buf, row, :], b_raw[:, row, :], ACT.Copy
                                         ).then_inc(b_hi_done, 1)

            def hs_high(c):
                act.wait_ge(h_done, c + 1)
                nc.scalar.activation(hs[:], h[:], ACT.Copy, scale=SCALING).then_inc(hs_hi_done, 1)

            b_high(0, 0)
            hs_high(0)
            for b in range(ROWS, BATCH):
                act.wait_ge(a_gathered[b], 16)
            with act.Fori(1, CHUNKS) as c:
                buf = bass.ds(act.snap(c & 1), 1)
                act.wait_ge(x_loaded, c * 16)
                for k in range(TILES):
                    x_high(buf, k)
                for row in range(ROWS):
                    act.wait_ge(h_done, c)
                    src = a_raw[:, bass.ds(c * ROWS + row, 1), :].rearrange(
                        "p a (k r) -> p k a r", k=TILES).to_broadcast([P, TILES, 4, R])
                    nc.scalar.activation(a_part(row, 0), src, ACT.Copy).then_inc(a_hi_done, 1)
                b_high(c, buf)
                hs_high(c)

        @block.vector
        def _(dve):
            dve.wait_ge(lane_made, 1)
            nc.vector.tensor_single_scalar(lane_r[:], lane[:], R - 1, op=ALU.bitwise_and).then_inc(lane_r_made, 1)
            dve.wait_ge(idx_loaded, 16)
            nc.vector.tensor_scalar(a_at[:], idx_sb[:], float(P), lane[:, 0:1], ALU.mult, ALU.add
                                    ).then_inc(at_made, 1)
            dve.wait_ge(lane_r_made, 1)
            nc.vector.tensor_scalar(b_at[:], idx_sb[:], float(R), lane_r[:, 0:1], ALU.mult, ALU.add
                                    ).then_inc(at_made, 1)
            dve.sem_inc(drained, GRANT)

            def w_low(half, k):
                dve.wait_ge(w_loaded[k], 16 * (half + 1))
                dve.wait_ge(w_hi_done, half * TILES + k + 1)
                nc.vector.tensor_tensor(w_piece(w_lo, half, k), w_raw[:, k, :],
                                        w_piece(w_hi, half, k).bitcast(F32), ALU.subtract).then_inc(w_lo_done, 1)

            for k in range(TILES):
                w_low(0, k)
                dve.wait_ge(x0_loaded[k], 16)
                dve.wait_ge(x_hi_done, k + 1)
                nc.vector.tensor_tensor(x_lo[:, 0, k, :], x_sb[:, 0, k, :], x_hi[:, 0, k, :].bitcast(F32),
                                        ALU.subtract).then_inc(x_lo_done, 1)
            for k in range(TILES):
                w_low(1, k)

            dve.wait_ge(bias_loaded, 16)
            def finish(c, buf):
                dve.wait_ge(h_done, c + 1)
                dve.wait_ge(hs_hi_done, c + 1)
                for q in (1, 3):
                    rows = slice(q * Q, (q + 1) * Q)
                    nc.vector.scalar_tensor_tensor(out=hs[rows, :], in0=h[rows, :], scalar=SCALING,
                                                   in1=hs[rows, :].bitcast(F32), op0=ALU.mult,
                                                   op1=ALU.subtract).then_inc(hs_lo_done, 1)
                for j in range(TILES):
                    dve.wait_ge(acc_done, c * TILES + j + 1)
                    tile = x_sb[:, buf, j, :]
                    nc.vector.scalar_tensor_tensor(out=tile, in0=acc[BANK[j]][:], scalar=bias_sb[:, j:j + 1],
                                                   in1=tile, op0=ALU.add, op1=ALU.add).then_inc(drained, 1)

            with dve.Fori(0, CHUNKS, 2) as c:
                finish(c, 0)
                finish(c + 1, 1)

        @block.tensor
        def _(pe):
            def take_bank(c, j):
                before = {4: 0, 7: 5}.get(j, j + 1 - TILES)
                pe.wait_ge(drained, c * TILES + GRANT + before)

            def main(buf, j, k):
                cols = slice(j * P, (j + 1) * P)
                bank = acc[BANK[j]][:]
                nc.tensor.matmul(bank, w_hi[:, k, cols], x_hi[:, buf, k, :], start=(k == 0), stop=False)
                nc.tensor.matmul(bank, w_hi[:, k, cols], x_lo[:, buf, k, :], start=False, stop=False)
                nc.tensor.matmul(bank, w_lo[:, k, cols], x_hi[:, buf, k, :], start=False, stop=False)

            def low_rank(buf, j):
                for row in range(ROWS):
                    tokens = slice(row * T, (row + 1) * T)
                    last = nc.tensor.matmul(acc[BANK[j]][:, tokens], b_rows[:, buf, row, j * P:(j + 1) * P],
                                            hs[:, tokens], start=False, stop=(row == ROWS - 1))
                last.then_inc(acc_done, 1)

            def chunk(c, buf):
                for k in range(TILES):
                    pe.wait_ge(w_hi_done, k + 1)
                    pe.wait_ge(w_lo_done, k + 1)
                    pe.wait_ge(x_hi_done, c * TILES + k + 1)
                    pe.wait_ge(x_lo_done, c * TILES + k + 1)
                    for j in range(HALF):
                        if k == 0:
                            take_bank(c, j)
                        main(buf, j, k)
                for row in range(ROWS):
                    tokens = slice(row * T, (row + 1) * T)
                    pe.wait_ge(a_hi_done, c * ROWS + row + 1)
                    pe.wait_ge(a_lo_done, c * ROWS + row + 1)
                    for k in range(TILES):
                        nc.tensor.matmul(h[:, tokens], a_cols[:, row, k, :], x_hi[:, buf, k, tokens],
                                         start=(k == 0), stop=False)
                        last = nc.tensor.matmul(h[:, tokens], a_cols[:, row, k, :], x_lo[:, buf, k, tokens],
                                                start=False, stop=(k == TILES - 1))
                last.then_inc(h_done, 1)
                for j in range(HALF, TILES):
                    take_bank(c, j)
                    for k in range(TILES):
                        if j == HALF:
                            pe.wait_ge(w_hi_done, TILES + k + 1)
                            pe.wait_ge(w_lo_done, TILES + k + 1)
                        main(buf, j, k)
                    if j == HALF:
                        pe.wait_ge(hs_lo_done, c * 2 + 2)
                        pe.wait_ge(b_hi_done, (c + 1) * ROWS)
                        pe.wait_ge(b_lo_done, (c + 1) * ROWS)
                        for first in range(HALF):
                            low_rank(buf, first)
                    low_rank(buf, j)

            with pe.Fori(0, CHUNKS, 2) as c:
                chunk(c, 0)
                chunk(c + 1, 1)


def build(nc, arrays, shapes):
    dts = {"f": F32, "i": I32}
    args = [nc.dram_tensor(name, a.shape, dts[a.dtype.kind], kind="ExternalInput").ap()
            for name, a in arrays.items()]
    out = nc.dram_tensor("out", shapes["out"], F32, kind="ExternalOutput").ap()
    lora_linear_kernel(nc, *args, out)


def kernel(x, itok_B_0_23, L0_cond_W, L0_cond_b, L0_cond_lora_As, L0_cond_lora_Bs):
    import concourse.bacc as bacc
    from concourse.bass_utils import run_bass_kernel_spmd

    x, idx, w, bias, lora_a, lora_b = (
        np.asarray(a) for a in (x, itok_B_0_23, L0_cond_W, L0_cond_b, L0_cond_lora_As, L0_cond_lora_Bs))
    arrays = {
        "x": np.ascontiguousarray(x.reshape(CHUNKS, N, P, TILES).transpose(0, 2, 3, 1)
                                  ).reshape(CHUNKS, P, TILES * N),
        "idx": np.ascontiguousarray(idx.reshape(1, BATCH)),
        "w": np.ascontiguousarray(w.reshape(P, 2, HALF, P, TILES).transpose(1, 4, 3, 2, 0)
                                  ).reshape(2, TILES, P, HALF * P),
        "bias": np.ascontiguousarray(bias.reshape(P, TILES)),
        "lora_a": np.ascontiguousarray(lora_a).reshape(SLOTS * P, TILES * R),
        "lora_b": np.ascontiguousarray(lora_b.reshape(SLOTS * R, P, TILES).transpose(0, 2, 1)
                                       ).reshape(SLOTS * R, D),
    }
    nc = bacc.Bacc("TRN2", target_bir_lowering=False, num_devices=1)
    build(nc, arrays, {"out": (CHUNKS, P, TILES * N)})
    r = run_bass_kernel_spmd(nc, [arrays], core_ids=[0])
    got = r.results[0]["out"].reshape(CHUNKS, P, TILES, N).transpose(0, 3, 1, 2)
    return np.ascontiguousarray(got).reshape(BATCH, T, D)
```
